# Optimizing a Trainium2 kernel written in Bass

```python
import numpy as np
import jax
import jax.numpy as jnp

def _softmax(x, axis=-1):
    return jax.nn.softmax(x, axis=axis)
def _gelu(x):
    return jax.nn.gelu(x, approximate=True)
def _silu(x):
    return jax.nn.silu(x)
def _sigmoid(x):
    return jax.nn.sigmoid(x)
def _layernorm(x, axis=-1, eps=1e-5):
    m = jnp.mean(x, axis=axis, keepdims=True)
    v = jnp.var(x, axis=axis, keepdims=True)
    return (x - m) / jnp.sqrt(v + eps)
def _scatter_add(tgt, idx, src, axis=0):
    return tgt.at[idx].add(src)
def _segment_sum(src, seg, n):
    return jax.ops.segment_sum(src, seg, n)

kernel_name = 'mk_conv_seq_d4_conv_nchw16_3e5210'

def setup_inputs(seed: int = 0):
    np.random.seed(seed)
    _w = jnp.asarray
    def _rec_inputs():
        import jax
        import jax.numpy as jnp
        _gk = jax.random.key(seed)
        x = -7.109e-05 + 0.9999 * jax.random.normal(jax.random.fold_in(_gk, 1), (8, 16, 512, 512), jnp.float32)
        return x
    x = _rec_inputs()
    def _L0_conv_setup():
        import jax, jax.numpy as jnp
        import numpy as np

        def _conv2d_same(x, w, b):
            y = jax.lax.conv_general_dilated(x, w, window_strides=(1, 1), padding=((1, 1), (1, 1)), dimension_numbers=('NCHW', 'OIHW', 'NCHW'))
            return y + b[None, :, None, None]
        key = jax.random.key(seed)
        ks = jax.random.split(key, 5)
        B, C, H, W = (16, 16, 512, 512)
        K = 3
        bound = float(np.sqrt(1.0 / (C * K * K)))
        x = jax.random.normal(ks[0], (B, C, H, W), dtype=jnp.float32)
        w1 = jax.random.uniform(ks[1], (C, C, K, K), minval=-bound, maxval=bound, dtype=jnp.float32)
        b1 = jax.random.uniform(ks[2], (C,), minval=-bound, maxval=bound, dtype=jnp.float32)
        w2 = jax.random.uniform(ks[3], (C, C, K, K), minval=-bound, maxval=bound, dtype=jnp.float32)
        b2 = jax.random.uniform(ks[4], (C,), minval=-bound, maxval=bound, dtype=jnp.float32)
        return {'x': x, 'w1': w1, 'b1': b1, 'w2': w2, 'b2': b2}
    _L0_conv_all = _L0_conv_setup()
    _L0_conv_in = {k: v for k, v in _L0_conv_all.items() if k in ('w1', 'b1', 'w2', 'b2', )}
    del _L0_conv_all

    def _L1_conv_setup():
        import jax, jax.numpy as jnp
        import numpy as np

        def _conv2d_same(x, w, b):
            y = jax.lax.conv_general_dilated(x, w, window_strides=(1, 1), padding=((1, 1), (1, 1)), dimension_numbers=('NCHW', 'OIHW', 'NCHW'))
            return y + b[None, :, None, None]
        key = jax.random.key(seed)
        ks = jax.random.split(key, 5)
        B, C, H, W = (16, 16, 512, 512)
        K = 3
        bound = float(np.sqrt(1.0 / (C * K * K)))
        x = jax.random.normal(ks[0], (B, C, H, W), dtype=jnp.float32)
        w1 = jax.random.uniform(ks[1], (C, C, K, K), minval=-bound, maxval=bound, dtype=jnp.float32)
        b1 = jax.random.uniform(ks[2], (C,), minval=-bound, maxval=bound, dtype=jnp.float32)
        w2 = jax.random.uniform(ks[3], (C, C, K, K), minval=-bound, maxval=bound, dtype=jnp.float32)
        b2 = jax.random.uniform(ks[4], (C,), minval=-bound, maxval=bound, dtype=jnp.float32)
        return {'x': x, 'w1': w1, 'b1': b1, 'w2': w2, 'b2': b2}
    _L1_conv_all = _L1_conv_setup()
    _L1_conv_in = {k: v for k, v in _L1_conv_all.items() if k in ('w1', 'b1', 'w2', 'b2', )}
    del _L1_conv_all

    def _L2_conv_setup():
        import jax, jax.numpy as jnp
        import numpy as np

        def _conv2d_same(x, w, b):
            y = jax.lax.conv_general_dilated(x, w, window_strides=(1, 1), padding=((1, 1), (1, 1)), dimension_numbers=('NCHW', 'OIHW', 'NCHW'))
            return y + b[None, :, None, None]
        key = jax.random.key(seed)
        ks = jax.random.split(key, 5)
        B, C, H, W = (16, 16, 512, 512)
        K = 3
        bound = float(np.sqrt(1.0 / (C * K * K)))
        x = jax.random.normal(ks[0], (B, C, H, W), dtype=jnp.float32)
        w1 = jax.random.uniform(ks[1], (C, C, K, K), minval=-bound, maxval=bound, dtype=jnp.float32)
        b1 = jax.random.uniform(ks[2], (C,), minval=-bound, maxval=bound, dtype=jnp.float32)
        w2 = jax.random.uniform(ks[3], (C, C, K, K), minval=-bound, maxval=bound, dtype=jnp.float32)
        b2 = jax.random.uniform(ks[4], (C,), minval=-bound, maxval=bound, dtype=jnp.float32)
        return {'x': x, 'w1': w1, 'b1': b1, 'w2': w2, 'b2': b2}
    _L2_conv_all = _L2_conv_setup()
    _L2_conv_in = {k: v for k, v in _L2_conv_all.items() if k in ('w1', 'b1', 'w2', 'b2', )}
    del _L2_conv_all

    def _L3_conv_setup():
        import jax, jax.numpy as jnp
        import numpy as np
        EPS = 1e-06
        key = jax.random.key(seed)
        k0, k1, k2 = jax.random.split(key, 3)
        B, H, S, MW = (1, 16, 2048, 32)
        x = jax.random.normal(k0, (B, H, S, S), dtype=jnp.float32)
        W1 = jax.random.normal(k1, (1, MW), dtype=jnp.float32)
        b1 = jnp.zeros((MW,), dtype=jnp.float32)
        W2 = jax.random.normal(k2, (MW, H), dtype=jnp.float32) * (1.0 / np.sqrt(MW))
        b2 = jnp.zeros((H,), dtype=jnp.float32)
        c = jnp.float32(0.1)
        L_multiplier = jnp.float32(1.0)
        init_L = jnp.float32(512.0)
        return {'x': x, 'W1': W1, 'b1': b1, 'W2': W2, 'b2': b2, 'c': c, 'L_multiplier': L_multiplier, 'init_L': init_L}
    _L3_conv_all = _L3_conv_setup()
    _L3_conv_in = {k: v for k, v in _L3_conv_all.items() if k in ('W1', 'b1', 'W2', 'b2', 'c', 'L_multiplier', 'init_L', )}
    del _L3_conv_all

    return {
        "x": x,
        "L0_conv_w1": _L0_conv_in["w1"],
        "L0_conv_b1": _L0_conv_in["b1"],
        "L0_conv_w2": _L0_conv_in["w2"],
        "L0_conv_b2": _L0_conv_in["b2"],
        "L1_conv_w1": _L1_conv_in["w1"],
        "L1_conv_b1": _L1_conv_in["b1"],
        "L1_conv_w2": _L1_conv_in["w2"],
        "L1_conv_b2": _L1_conv_in["b2"],
        "L2_conv_w1": _L2_conv_in["w1"],
        "L2_conv_b1": _L2_conv_in["b1"],
        "L2_conv_w2": _L2_conv_in["w2"],
        "L2_conv_b2": _L2_conv_in["b2"],
        "L3_conv_W1": _L3_conv_in["W1"],
        "L3_conv_b1": _L3_conv_in["b1"],
        "L3_conv_W2": _L3_conv_in["W2"],
        "L3_conv_b2": _L3_conv_in["b2"],
        "L3_conv_c": _L3_conv_in["c"],
        "L3_conv_L_multiplier": _L3_conv_in["L_multiplier"],
        "L3_conv_init_L": _L3_conv_in["init_L"],
    }

def reference(x, L0_conv_w1, L0_conv_b1, L0_conv_w2, L0_conv_b2, L1_conv_w1, L1_conv_b1, L1_conv_w2, L1_conv_b2, L2_conv_w1, L2_conv_b1, L2_conv_w2, L2_conv_b2, L3_conv_W1, L3_conv_b1, L3_conv_W2, L3_conv_b2, L3_conv_c, L3_conv_L_multiplier, L3_conv_init_L):
    import jax
    import jax.numpy as jnp
    def _L0_conv_ref(x, w1, b1, w2, b2):
        import jax, jax.numpy as jnp
        import numpy as np

        def _conv2d_same(x, w, b):
            y = jax.lax.conv_general_dilated(x, w, window_strides=(1, 1), padding=((1, 1), (1, 1)), dimension_numbers=('NCHW', 'OIHW', 'NCHW'))
            return y + b[None, :, None, None]
        out = _conv2d_same(x, w1, b1)
        out = jax.nn.relu(out)
        out = _conv2d_same(out, w2, b2)
        return out + x

    def _L1_conv_ref(x, w1, b1, w2, b2):
        import jax, jax.numpy as jnp
        import numpy as np

        def _conv2d_same(x, w, b):
            y = jax.lax.conv_general_dilated(x, w, window_strides=(1, 1), padding=((1, 1), (1, 1)), dimension_numbers=('NCHW', 'OIHW', 'NCHW'))
            return y + b[None, :, None, None]
        out = _conv2d_same(x, w1, b1)
        out = jax.nn.relu(out)
        out = _conv2d_same(out, w2, b2)
        return out + x

    def _L2_conv_ref(x, w1, b1, w2, b2):
        import jax, jax.numpy as jnp
        import numpy as np

        def _conv2d_same(x, w, b):
            y = jax.lax.conv_general_dilated(x, w, window_strides=(1, 1), padding=((1, 1), (1, 1)), dimension_numbers=('NCHW', 'OIHW', 'NCHW'))
            return y + b[None, :, None, None]
        out = _conv2d_same(x, w1, b1)
        out = jax.nn.relu(out)
        out = _conv2d_same(out, w2, b2)
        return out + x

    def _L3_conv_ref(x, W1, b1, W2, b2, c, L_multiplier, init_L):
        import jax, jax.numpy as jnp
        import numpy as np
        EPS = 1e-06
        S = x.shape[-1]
        idx = jnp.arange(S)
        rel = jnp.tril(idx[:, None] - idx[None, :]).astype(jnp.float32)
        threshold = jnp.abs(L_multiplier * init_L)
        pos = jnp.maximum(rel.max(axis=-1), threshold)[:, None]
        nd = jnp.log(jnp.abs(c * rel) + 1.0) / (jnp.log(jnp.abs(c * pos) + 1.0) + EPS)
        nd = nd.astype(x.dtype)
        h = jax.nn.relu(nd[..., None] * W1[0] + b1)
        bias = jnp.einsum('qkm,mh->qkh', h, W2) + b2
        return x + bias.transpose(2, 0, 1)[None]

    def _gn(v, G=8, eps=1e-5):
        B_, C_, H_, W_ = v.shape
        g = v.reshape(B_, G, C_ // G, H_, W_)
        m = jnp.mean(g, axis=(2, 3, 4), keepdims=True)
        s = jnp.var(g, axis=(2, 3, 4), keepdims=True)
        return ((g - m) / jnp.sqrt(s + eps)).reshape(v.shape)

    def _ln_c(v, eps=1e-6):
        m = jnp.mean(v, axis=1, keepdims=True)
        s = jnp.var(v, axis=1, keepdims=True)
        return (v - m) / jnp.sqrt(s + eps)

    def _ln_t(v, eps=1e-5):
        m = jnp.mean(v, axis=-1, keepdims=True)
        s = jnp.var(v, axis=-1, keepdims=True)
        return (v - m) / jnp.sqrt(s + eps)

    def _to_tokens(v):
        B_, C_, H_, W_ = v.shape
        return v.reshape(B_, C_, H_ * W_).transpose(0, 2, 1)
    def _from_tokens(t, like):
        B_, C_, H_, W_ = like.shape
        return t.transpose(0, 2, 1).reshape(B_, C_, H_, W_)

    x = _L0_conv_ref(x, L0_conv_w1, L0_conv_b1, L0_conv_w2, L0_conv_b2)
    x = _L1_conv_ref(x, L1_conv_w1, L1_conv_b1, L1_conv_w2, L1_conv_b2)
    x = _L2_conv_ref(x, L2_conv_w1, L2_conv_b1, L2_conv_w2, L2_conv_b2)
    x = _L3_conv_ref(x, L3_conv_W1, L3_conv_b1, L3_conv_W2, L3_conv_b2, L3_conv_c, L3_conv_L_multiplier, L3_conv_init_L)
    return x


_drawn_inputs = setup_inputs


def setup_inputs(seed=0):
    import zlib

    import numpy as np

    out = dict(_drawn_inputs(seed))
    spreads = {'L3_conv_b1': (0.0, 0.1), 'L3_conv_b2': (0.0, 0.1)}
    factors = {'L0_conv_b1': 3.743, 'L1_conv_b1': 3.955, 'L2_conv_b1': 4.047}
    for name, (base, spread) in spreads.items():
        noise = np.random.default_rng([zlib.crc32(name.encode()), seed]).standard_normal(out[name].shape)
        drawn = base * np.exp(spread * noise) if base else spread * noise
        out[name] = jnp.asarray(drawn.astype(out[name].dtype))
    for name, factor in factors.items():
        out[name] = (out[name] * factor).astype(out[name].dtype)
    return out
```

```python
from contextlib import ExitStack

import numpy as np

import concourse.bass as bass
from concourse import mybir

ALU = mybir.AluOpType
ACT = mybir.ActivationFunctionType
F32 = mybir.dt.float32
F32R = mybir.dt.float32r

P = 128
IMAGES, CH, ROWS, COLS = 8, 16, 512, 512
BR, BC = 4, 2
QUAD = BC * CH
PAIRS = COLS // BC
BLOCKS = ROWS // BR
NT = BLOCKS // 2
TILES = IMAGES * NT
CONVS = 6
WIDTH = PAIRS + 4
HIDDEN = 32
EPS = 1e-6
UNROLL = 4
XRING, ARING, ORING, PRING = 4, 2, 2, 4

FIRST = [(c + 1) // 2 for c in range(CONVS)]
LAST = [(2 * TILES - 1 + c + 1) // 2 for c in range(CONVS)]
STEPS = LAST[5] + CONVS
RAMP = 3 * UNROLL
TOP_Q, BOTTOM_Q = slice(0, QUAD), slice(QUAD, 2 * QUAD)
FIRST_ROW, LAST_ROW = slice(0, QUAD), slice((BR - 1) * QUAD, BR * QUAD)


def conv_kernel(nc, x, weights, conv_bias, w1, b1, w2, out_bias, scalars, distance, row_index,
                edge, out):
    table = nc.dram_tensor("position_bias", (NT, P, 2, PAIRS), F32, kind="Internal").ap()

    with ExitStack() as ctx:
        def sb(name, shape, dt=F32):
            return ctx.enter_context(nc.sbuf_tensor(name, shape, dt))

        def sem(name):
            return ctx.enter_context(nc.semaphore(name))

        w_raw = sb("w_raw", [P, CONVS, 3, P])
        w_high = sb("w_high", [P, CONVS, 3, P], F32R)
        w_low = sb("w_low", [P, CONVS, 3, P], F32R)
        bias_sb = sb("conv_bias_sb", [P, CONVS])
        edge_sb = sb("edge_sb", [P, 2, 2])
        zeros = sb("zeros", [P, 2, WIDTH])
        resid = {L: sb(f"resid{L}", [P, XRING, 2, PAIRS]) for L in (0, 2, 4)}
        relu = {L: sb(f"relu{L}", [P, 2, PAIRS + 1]) for L in (1, 3, 5)}
        split = [sb(f"split{L}", [P, ARING, 2, 2, WIDTH], F32R) for L in range(CONVS)]
        halo = [sb(f"halo{L}", [P, 2, 2, WIDTH], F32R) for L in range(CONVS)]
        pos_tile = sb("pos_tile", [P, ORING, 2, PAIRS])
        out_tile = sb("out_tile", [P, ORING, 2, PAIRS])
        dist_sb = sb("dist_sb", [P, 2, 2 * PAIRS])
        row_sb = sb("row_sb", [P, 2, BLOCKS])
        w2_sb = sb("w2_sb", [P, 2, P])
        small = sb("small", [P, 6])
        magnitude = sb("magnitude", [P, 3])
        hidden = sb("hidden", [P, 2, 2, 2, PAIRS])
        ps = ctx.enter_context(nc.psum_tensor("ps", [P, 2 * PRING, 512], F32))

        consts_in, weights_in = sem("consts_in"), sem("weights_in")
        w_high_made, w_low_made, cleared = sem("w_high_made"), sem("w_low_made"), sem("cleared")
        prep_v, prep_a = sem("prep_v"), sem("prep_a")
        hidden_made, pos_summed = sem("hidden_made"), sem("pos_summed")
        pos_made, pos_stored = sem("pos_made"), [sem(f"pos_stored{i}") for i in range(2)]
        x_in = [sem(f"x_in{i}") for i in range(XRING)]
        pos_in = [sem(f"pos_in{i}") for i in range(ORING)]
        out_stored = [sem(f"out_stored{i}") for i in range(ORING)]
        conv_done = [sem(f"conv_done{c}") for c in range(CONVS)]
        level_made = [None] + [sem(f"level_made{L}") for L in range(1, CONVS + 1)]
        edges_cut = {L: sem(f"edges_cut{L}") for L in (1, 3, 5)}
        high_made = [sem(f"high_made{L}") for L in range(CONVS)]
        low_made = [sem(f"low_made{L}") for L in range(CONVS)]
        top_in = [sem(f"top_in{L}") for L in range(CONVS)]
        bottom_in = [sem(f"bottom_in{L}") for L in range(CONVS)]
        halo_made = [sem(f"halo_made{L}") for L in range(CONVS)]
        out_made = sem("out_made")

        block = ctx.enter_context(nc.Block())

        def conv_runs(c, t):
            return not isinstance(t, int) or FIRST[c] <= t <= LAST[c]

        def level_has(L, u):
            return (not isinstance(u, int) or 0 <= u < TILES) if L == 0 else conv_runs(L - 1, u)

        def nth(L, u):
            return u + 1 if L == 0 else u - FIRST[L - 1] + 1

        def nth_conv(c, t):
            return t - FIRST[c] + 1

        def bank(c, phase):
            return 2 * ((CONVS * phase + CONVS - 1 - c) % PRING)

        def steps(engine, step):
            for s in range(RAMP):
                step(s, s % UNROLL)
            with engine.Fori(RAMP // UNROLL, TILES // UNROLL - 1) as i:
                for k in range(UNROLL):
                    step(i * UNROLL + k, k)
            for s in range(TILES - UNROLL, STEPS):
                step(s, s % UNROLL)

        @block.sync
        def _(sp):
            sp.dma_start(w_raw[:, :, :, :], weights).then_inc(weights_in, 16)
            for dst, src in ((dist_sb[:, :, :], distance), (row_sb[:, :, :], row_index),
                             (w2_sb[:, :, :], w2), (small[:, 0:1], w1), (small[:, 1:2], b1),
                             (small[:, 2:3], out_bias), (small[:, 3:6], scalars),
                             (bias_sb[:, :], conv_bias), (edge_sb[:, :, :], edge)):
                sp.dma_start(dst, src).then_inc(consts_in, 16)
            for u in range(XRING):
                sp.dma_start(resid[0][:, u, :, :], x[u]).then_inc(x_in[u], 16)

            with sp.Fori(0, NT // 2) as i:
                for k in range(2):
                    sp.wait_ge(pos_made, i * 2 + (k + 1))
                    sp.dma_start(table[i * 2 + k], out_tile[:, k, :, :]).then_inc(pos_stored[k], 16)
            for k in range(2):
                sp.wait_ge(pos_stored[k], 16 * (NT // 2))
            sp.wait_ge(cleared, 1)

            def top(L, s, phase, j):
                u = s + 1 - L
                if not conv_runs(L, u):
                    return
                if conv_runs(L, u - 1):
                    sp.wait_ge(conv_done[L], nth_conv(L, u - 1))
                elif level_has(L, u - 1):
                    sp.wait_ge(low_made[L], nth(L, u - 1))
                src = split[L][LAST_ROW, (phase - L) % ARING, :, :, :].bitcast(F32)
                dst = halo[L][TOP_Q, :, :, :].bitcast(F32)
                if j is not None and (j + 1 - L) % NT == (L + 1) // 2:
                    cut = 1 - L % 2
                    sp.dma_start(dst[:, :, cut, :], zeros[TOP_Q, :, :]).then_inc(top_in[L], 16)
                    sp.dma_start(dst[:, :, 1 - cut, :], src[:, :, 1 - cut, :]).then_inc(top_in[L], 16)
                else:
                    sp.dma_start(dst, src).then_inc(top_in[L], 32)

            def bottom(L, s, phase, j):
                u = s + 1 - L
                if not conv_runs(L, u):
                    return
                if conv_runs(L, u - 1):
                    sp.wait_ge(conv_done[L], nth_conv(L, u - 1))
                if level_has(L, u):
                    sp.wait_ge(low_made[L], nth(L, u))
                src = split[L][FIRST_ROW, (phase + 1 - L) % ARING, :, :, :].bitcast(F32)
                dst = halo[L][BOTTOM_Q, :, :, :].bitcast(F32)
                if j is not None and (j + 1 - L) % NT == L // 2:
                    cut = L % 2
                    sp.dma_start(dst[:, :, cut, :], zeros[BOTTOM_Q, :, :]).then_inc(bottom_in[L], 16)
                    sp.dma_start(dst[:, :, 1 - cut, :], src[:, :, 1 - cut, :]).then_inc(bottom_in[L], 16)
                else:
                    sp.dma_start(dst, src).then_inc(bottom_in[L], 32)

            def step(s, phase, j, table_tile):
                static = isinstance(s, int)
                if not static or CONVS + 1 <= s < STEPS - 1:
                    if not static or s - CONVS - 1 >= ORING:
                        sp.wait_ge(out_made, s - (CONVS + 2))
                    n = (j - CONVS - 1) % NT if j is not None else table_tile
                    sp.dma_start(pos_tile[:, (phase + 1) % ORING, :, :], table[n]).then_inc(
                        pos_in[(phase + 1) % ORING], 16)
                for c in reversed(range(CONVS)):
                    top(c, s, phase, j)
                    if c + 2 < CONVS:
                        bottom(c + 2, s, phase, j)
                    if c == 3 and conv_runs(5, s - 5):
                        sp.wait_ge(out_made, nth_conv(5, s - 5))
                        sp.dma_start(out[s - 8], out_tile[:, phase % ORING, :, :]).then_inc(
                            out_stored[phase % ORING], 16)
                    if c == 0 and (not static or XRING <= s + 2 < TILES):
                        sp.wait_ge(level_made[2], nth(2, s - 1))
                        sp.dma_start(resid[0][:, (phase + 2) % XRING, :, :], x[s + 2]).then_inc(
                            x_in[(phase + 2) % XRING], 16)
                bottom(1, s, phase, j)
                bottom(0, s, phase, j)

            top(0, -1, UNROLL - 1, NT - 1)
            bottom(0, -1, UNROLL - 1, NT - 1)
            for s in range(RAMP):
                step(s, s % UNROLL, s, None)

            def middle(base, groups):
                with sp.Fori(RAMP // UNROLL, groups) as i:
                    for k in range(UNROLL):
                        step(base + i * UNROLL + k, k, None, i * UNROLL + (k - CONVS - 1))

            def image_steps(base, groups):
                for j in range(RAMP):
                    step(base + j, j % UNROLL, j, None)
                middle(base, groups)

            middle(0, NT // UNROLL - 1)
            for j in range(NT - UNROLL, NT):
                step(j, j % UNROLL, j, None)
            with sp.Fori(1, IMAGES - 1) as image:
                image_steps(image * NT, NT // UNROLL - 1)
                for j in range(NT - UNROLL, NT):
                    step(image * NT + j, j % UNROLL, j, None)
            image_steps(TILES - NT, NT // UNROLL - 1)
            for s in range(TILES - UNROLL, STEPS):
                step(s, s % UNROLL, s % NT, None)
            for k in range(ORING):
                sp.wait_ge(out_stored[k], 16 * (TILES // ORING))

        @block.tensor
        def _(pe):
            pe.wait_ge(consts_in, 16 * 9)

            def second_layer(T, k, first):
                pe.wait_ge(hidden_made, T + 1)
                if not first:
                    pe.wait_ge(pos_made, T - 1)
                for b in range(2):
                    for g in range(2):
                        mm = pe.matmul(ps[:, 2 * k + b, 0:PAIRS], w2_sb[:, g, :],
                                       hidden[:, k, b, g, :], start=(g == 0), stop=(g == 1))
                mm.then_inc(pos_summed, 1)

            for k in range(2):
                second_layer(k, k, True)
            with pe.Fori(1, NT // 2) as i:
                for k in range(2):
                    second_layer(i * 2 + k, k, False)
            pe.wait_ge(w_low_made, 1)
            pe.wait_ge(pos_made, NT)

            def conv(c, s, phase):
                t = s - c
                if not conv_runs(c, t):
                    return
                if level_has(c, t):
                    pe.wait_ge(low_made[c], nth(c, t))
                before, at = c, s
                for _ in range(3):
                    before, at = (before + 4, at) if before < 2 else (before - 2, at - 1)
                    if conv_runs(before, at - before):
                        pe.wait_ge(level_made[before + 1], nth_conv(before, at - before))
                        break
                n = PAIRS + 2 if c % 2 == 0 else PAIRS
                first = bank(c, phase)
                slots = [((phase - c - 1) % ARING, 1), ((phase - c) % ARING, 0)]
                for shift in range(2):
                    for part, w in ((0, w_high), (0, w_low), (1, w_high)):
                        for b, (slot, blk) in enumerate(slots):
                            pe.matmul(ps[:, first + b, 0:n], w[:, c, shift, :],
                                      split[c][:, slot, part, blk, shift:shift + n],
                                      start=(shift == 0 and part == 0 and w is w_high), stop=False)
                pe.wait_ge(halo_made[c], nth_conv(c, t))
                for k, (part, w) in enumerate(((0, w_high), (0, w_low), (1, w_high))):
                    for b in range(2):
                        mm = pe.matmul(ps[:, first + b, 0:n], w[:, c, 2, :],
                                       halo[c][:, part, b, 0:n], start=False, stop=(k == 2))
                mm.then_inc(conv_done[c], 1)

            def step(s, phase):
                for c in reversed(range(CONVS)):
                    conv(c, s, phase)

            steps(pe, step)

        @block.scalar
        def _(act):
            act.wait_ge(weights_in, 16)
            nc.scalar.activation(w_high[:, :, :, :], w_raw[:, :, :, :], ACT.Copy).then_inc(w_high_made, 1)
            act.wait_ge(prep_v, 5)
            nc.scalar.activation(dist_sb[:, :, :], dist_sb[:, :, :], ACT.Ln, bias=1.0).then_inc(prep_a, 1)
            nc.scalar.activation(row_sb[:, :, :], row_sb[:, :, :], ACT.Ln, bias=1.0).then_inc(prep_a, 1)
            act.wait_ge(prep_v, 8)
            def hidden_tile(T, k, first):
                if not first:
                    act.wait_ge(pos_summed, T - 1)
                for b in range(2):
                    for g in range(2):
                        h = nc.scalar.activation(
                            hidden[:, k, b, g, :],
                            dist_sb[:, g, bass.ds(2 * (BLOCKS - 1) - (T * 4 + 2 * b), PAIRS)],
                            ACT.Relu, bias=small[:, 1:2],
                            scale=row_sb[:, g, bass.ds(T * 2 + b, 1)])
                h.then_inc(hidden_made, 1)

            for k in range(2):
                hidden_tile(k, k, True)
            with act.Fori(1, NT // 2) as i:
                for k in range(2):
                    hidden_tile(i * 2 + k, k, False)

            def split_input(u, phase):
                if not level_has(0, u):
                    return
                act.wait_ge(x_in[phase % XRING], load_count(u, phase))
                if conv_runs(0, u - 1):
                    act.wait_ge(conv_done[0], nth_conv(0, u - 1))
                nc.scalar.activation(split[0][:, phase % ARING, 0, :, 1:PAIRS + 1],
                                     resid[0][:, phase % XRING, :, :], ACT.Copy).then_inc(high_made[0], 1)

            def load_count(u, phase):
                return 16 * (u // XRING + 1) if isinstance(u, int) else (u - phase % XRING) * 4 + 16

            def shift_halo(L, u):
                if not conv_runs(L, u):
                    return
                act.wait_ge(top_in[L], nth_conv(L, u) * 32)
                act.wait_ge(bottom_in[L], nth_conv(L, u) * 32)
                nc.scalar.activation(
                    halo[L][64:128, :, :, 0:WIDTH - 1].rearrange("p h b w -> p (h b) w"),
                    halo[L][0:64, :, :, 1:WIDTH].rearrange("p h b w -> p (h b) w").bitcast(F32),
                    ACT.Copy).then_inc(halo_made[L], 1)

            def step(s, phase):
                for c in (4, 3, 2, 1, 0):
                    if c % 2 == 0 and conv_runs(c, s - c):
                        L = c + 1
                        act.wait_ge(conv_done[c], nth_conv(c, s - c))
                        if conv_runs(c, s - c - 1):
                            act.wait_ge(low_made[L], nth_conv(c, s - c - 1))
                        first = bank(c, phase)
                        nc.scalar.activation(relu[L][:, :, :], ps[:, first:first + 2, 0:PAIRS + 1], ACT.Relu,
                                             bias=bias_sb[:, c:c + 1]).then_inc(level_made[L], 1)
                    if c == 0:
                        split_input(s + 1, phase + 1)
                    if c + 2 < CONVS:
                        shift_halo(c + 2, s - c - 1)
                shift_halo(1, s)
                shift_halo(0, s + 1)

            act.wait_ge(cleared, 1)
            split_input(0, 0)
            shift_halo(0, 0)
            steps(act, step)

        @block.vector
        def _(dve):
            nc.vector.memset(zeros[:, :, :], 0.0)
            for L in range(CONVS):
                nc.vector.memset(halo[L][:, :, :, :].bitcast(F32), 0.0)
                last = nc.vector.memset(split[L][:, :, :, :, :].bitcast(F32), 0.0)
            last.then_inc(cleared, 1)
            dve.wait_ge(cleared, 1)
            dve.wait_ge(consts_in, 16 * 9)
            product, abs_c, threshold = magnitude[:, 0:1], magnitude[:, 1:2], magnitude[:, 2:3]
            nc.vector.tensor_tensor(product, small[:, 4:5], small[:, 5:6], ALU.mult).then_inc(prep_v, 1)
            nc.vector.scalar_tensor_tensor(out=abs_c, in0=small[:, 3:4], scalar=-1.0, in1=small[:, 3:4],
                                           op0=ALU.mult, op1=ALU.max).then_inc(prep_v, 1)
            dve.wait_ge(prep_v, 2)
            nc.vector.scalar_tensor_tensor(out=threshold, in0=product, scalar=-1.0, in1=product,
                                           op0=ALU.mult, op1=ALU.max).then_inc(prep_v, 1)
            nc.vector.tensor_scalar(dist_sb[:, :, :], dist_sb[:, :, :], abs_c, None,
                                    ALU.mult).then_inc(prep_v, 1)
            dve.wait_ge(prep_v, 3)
            nc.vector.tensor_scalar(row_sb[:, :, :], row_sb[:, :, :], threshold, abs_c,
                                    ALU.max, ALU.mult).then_inc(prep_v, 1)
            dve.wait_ge(prep_a, 2)
            nc.vector.tensor_scalar(row_sb[:, :, :], row_sb[:, :, :], EPS, None, ALU.add).then_inc(prep_v, 1)
            dve.wait_ge(prep_v, 6)
            nc.vector.reciprocal(row_sb[:, :, :], row_sb[:, :, :]).then_inc(prep_v, 1)
            dve.wait_ge(prep_v, 7)
            nc.vector.tensor_scalar(row_sb[:, :, :], row_sb[:, :, :], small[:, 0:1], None,
                                    ALU.mult).then_inc(prep_v, 1)
            dve.wait_ge(w_high_made, 1)
            nc.vector.tensor_tensor(w_low[:, :, :, :], w_raw[:, :, :, :], w_high[:, :, :, :].bitcast(F32),
                                    ALU.subtract).then_inc(w_low_made, 1)

            def pos_tile_out(T, k, group):
                dve.wait_ge(pos_summed, T + 1)
                if group is not None:
                    dve.wait_ge(pos_stored[k], group * 16)
                nc.vector.tensor_scalar(out_tile[:, k, :, :], ps[:, 2 * k:2 * k + 2, 0:PAIRS],
                                        small[:, 2:3], None, ALU.add).then_inc(pos_made, 1)

            for k in range(2):
                pos_tile_out(k, k, None)
            with dve.Fori(1, NT // 2) as i:
                for k in range(2):
                    pos_tile_out(i * 2 + k, k, i)
            for k in range(2):
                dve.wait_ge(pos_stored[k], 16 * (NT // 2))

            def low(L, phase, src, dst_cols):
                nc.vector.tensor_tensor(
                    split[L][:, phase % ARING, 1, :, dst_cols], src,
                    split[L][:, phase % ARING, 0, :, dst_cols].bitcast(F32), ALU.subtract
                ).then_inc(low_made[L], 1)

            def relu_level(L, s, phase):
                u, c = s + 1 - L, L - 1
                if not conv_runs(c, u):
                    return
                dve.wait_ge(level_made[L], nth(L, u))
                ends = relu[L][:, :, 0:PAIRS + 1:PAIRS]
                nc.vector.tensor_tensor(ends, ends, edge_sb[:, :, :], ALU.min).then_inc(edges_cut[L], 1)
                if L < CONVS and conv_runs(L, s - L):
                    dve.wait_ge(conv_done[L], nth_conv(L, s - L))
                dve.wait_ge(edges_cut[L], nth(L, u))
                nc.vector.tensor_copy(split[L][:, (phase + 1 - L) % ARING, 0, :, 0:PAIRS + 1],
                                      relu[L][:, :, :]).then_inc(high_made[L], 1)
                dve.wait_ge(high_made[L], nth(L, u))
                low(L, phase + 1 - L, relu[L][:, :, :], slice(0, PAIRS + 1))

            def residual_level(L, s, phase):
                u, c = s + 1 - L, L - 1
                if not conv_runs(c, u):
                    return
                dve.wait_ge(conv_done[c], nth(L, u))
                first = bank(c, phase)
                slot = (phase + 1 - L) % XRING
                if L == 2:
                    dve.wait_ge(high_made[0], nth(0, u - 1))
                    dve.wait_ge(low_made[0], nth(0, u - 1))
                else:
                    dve.wait_ge(level_made[L - 2], nth(L - 2, u - 1))
                nc.vector.scalar_tensor_tensor(
                    out=resid[L][:, slot, :, :], in0=ps[:, first:first + 2, 0:PAIRS],
                    scalar=bias_sb[:, c:c + 1], in1=resid[L - 2][:, (slot - 1) % XRING, :, :],
                    op0=ALU.add, op1=ALU.add).then_inc(level_made[L], 1)
                if conv_runs(L, s - L):
                    dve.wait_ge(conv_done[L], nth_conv(L, s - L))
                dve.wait_ge(level_made[L], nth(L, u))
                nc.vector.tensor_copy(split[L][:, (phase + 1 - L) % ARING, 0, :, 1:PAIRS + 1],
                                      resid[L][:, slot, :, :]).then_inc(high_made[L], 1)
                dve.wait_ge(high_made[L], nth(L, u))
                low(L, phase + 1 - L, resid[L][:, slot, :, :], slice(1, PAIRS + 1))

            def result(s, phase, pairs_before):
                u = s - 5
                if not conv_runs(5, u):
                    return
                dve.wait_ge(conv_done[5], nth_conv(5, u))
                dve.wait_ge(level_made[4], nth(4, u - 1))
                if pairs_before is not None:
                    dve.wait_ge(out_stored[phase % ORING], pairs_before * 16)
                first = bank(5, phase)
                tile = out_tile[:, phase % ORING, :, :]
                nc.vector.scalar_tensor_tensor(
                    out=tile, in0=ps[:, first:first + 2, 0:PAIRS], scalar=bias_sb[:, 5:6],
                    in1=resid[4][:, (phase - 6) % XRING, :, :], op0=ALU.add, op1=ALU.add
                ).then_inc(level_made[6], 1)

            def add_position(s, phase, nth_load):
                u = s - 5
                if not conv_runs(5, u):
                    return
                tile = out_tile[:, phase % ORING, :, :]
                dve.wait_ge(pos_in[phase % ORING], nth_load * 16)
                dve.wait_ge(level_made[6], nth(6, u))
                nc.vector.tensor_tensor(tile, tile, pos_tile[:, phase % ORING, :, :], ALU.add).then_inc(out_made, 1)

            def step(s, phase, half):
                n = half - 4
                result(s, phase, n if not isinstance(n, int) or n > 0 else None)
                add_position(s, phase, n + 1)
                relu_level(5, s, phase)
                residual_level(4, s, phase)
                relu_level(3, s, phase)
                residual_level(2, s, phase)
                relu_level(1, s, phase)
                if level_has(0, s + 1):
                    dve.wait_ge(high_made[0], nth(0, s + 1))
                    low(0, phase + 1, resid[0][:, (phase + 1) % XRING, :, :], slice(1, PAIRS + 1))

            dve.wait_ge(high_made[0], 1)
            low(0, 0, resid[0][:, 0, :, :], slice(1, PAIRS + 1))
            for s in range(RAMP):
                step(s, s % UNROLL, s // 2)
            with dve.Fori(RAMP // UNROLL, TILES // UNROLL - 1) as i:
                for k in range(UNROLL):
                    step(i * UNROLL + k, k, i * 2 + k // 2)
            for s in range(TILES - UNROLL, STEPS):
                step(s, s % UNROLL, s // 2)


def band(w):
    w = np.transpose(w, (2, 3, 1, 0))
    m = np.zeros((3, BR, BC, CH, BR, BC, CH), w.dtype)
    h = m[2].reshape(2, 2, BC, CH, BR, BC, CH)
    for shift in range(2):
        for ci in range(BC):
            for co in range(BC):
                dx = ci - co + 2 * shift
                if not 0 <= dx <= 2:
                    continue
                for ro in range(BR):
                    for ri in range(max(0, ro - 1), min(BR, ro + 2)):
                        m[shift, ri, ci, :, ro, co, :] = w[ri - ro + 1, dx]
                h[shift, 0, ci, :, 0, co, :] = w[0, dx]
                h[shift, 1, ci, :, BR - 1, co, :] = w[2, dx]
    return m.reshape(3, P, P).transpose(1, 0, 2)


def kernel(**inputs):
    import concourse.bacc as bacc
    from concourse.bass_utils import run_bass_kernel_spmd

    a = {k: np.asarray(v) for k, v in inputs.items()}
    f32 = np.float32

    def tiled(v):
        v = v.reshape(IMAGES, CH, NT, 2, BR, PAIRS, BC).transpose(0, 2, 4, 6, 1, 3, 5)
        return np.ascontiguousarray(v).reshape(TILES, P, 2, PAIRS)

    convs = [(a[f"L{n}_conv_w{i}"], a[f"L{n}_conv_b{i}"]) for n in range(3) for i in (1, 2)]
    pixels = 4
    w2 = np.zeros((2, BC, HIDDEN, 2, BR, BC, CH), f32)
    for g in range(2):
        for r in range(2):
            for c in range(BC):
                w2[r, c, :, g, 2 * g + r, c, :] = a["L3_conv_W2"]
    m = np.arange(2 * PAIRS)
    r, c, g = np.arange(2)[:, None, None, None], np.arange(BC)[:, None, None], np.arange(2)[:, None]
    distance = np.maximum(2 * (2 * (BLOCKS - 1) - m) + 2 * g + r - c, 0)
    distance = np.repeat(distance.reshape(pixels, 1, 2, 2 * PAIRS), HIDDEN, 1)
    rows = BR * np.arange(BLOCKS) + 2 * g + r + 0 * c
    rows = np.repeat(rows.reshape(pixels, 1, 2, BLOCKS), HIDDEN, 1)
    edge = np.full((BR, BC, CH, 2, 2), np.finfo(f32).max, f32)
    edge[:, 0, :, :, 0] = 0
    edge[:, 1, :, :, 1] = 0
    arrays = {
        "x": tiled(a["x"]),
        "weights": np.stack([band(w) for w, _ in convs], 1),
        "conv_bias": np.stack([np.tile(b, BR * BC) for _, b in convs], 1),
        "w1": np.tile(a["L3_conv_W1"].reshape(HIDDEN), pixels).reshape(P, 1),
        "b1": np.tile(a["L3_conv_b1"], pixels).reshape(P, 1),
        "w2": w2.reshape(P, 2, P),
        "out_bias": np.tile(a["L3_conv_b2"], BR * BC).reshape(P, 1),
        "scalars": np.tile(np.stack([a["L3_conv_c"], a["L3_conv_L_multiplier"], a["L3_conv_init_L"]])
                           .reshape(1, 3), (P, 1)),
        "distance": distance.reshape(P, 2, 2 * PAIRS).astype(f32),
        "row_index": rows.reshape(P, 2, BLOCKS).astype(f32),
        "edge": edge.reshape(P, 2, 2),
    }
    nc = bacc.Bacc("TRN2", target_bir_lowering=False, num_devices=1)
    aps = {}
    for name, v in arrays.items():
        arrays[name] = v = np.ascontiguousarray(v)
        aps[name] = nc.dram_tensor(name, v.shape, mybir.dt.from_np(v.dtype), kind="ExternalInput").ap()
    out = nc.dram_tensor("out", (TILES, P, 2, PAIRS), F32, kind="ExternalOutput").ap()
    conv_kernel(nc, out=out, **aps)
    result = run_bass_kernel_spmd(nc, [arrays], core_ids=[0]).results[0]["out"]
    result = np.asarray(result).reshape(IMAGES, NT, BR, BC, CH, 2, PAIRS).transpose(0, 4, 1, 5, 2, 6, 3)
    return result.reshape(1, IMAGES, CH, ROWS, COLS)[0]
```

```python
from contextlib import ExitStack

import numpy as np

import concourse.bass as bass
from concourse import mybir

ALU = mybir.AluOpType
ACT = mybir.ActivationFunctionType
F32 = mybir.dt.float32
F32R = mybir.dt.float32r

P = 128
IMAGES, CH, ROWS, COLS = 8, 16, 512, 512
BR, BC = 4, 2
QUAD = BC * CH
PAIRS = COLS // BC
BLOCKS = ROWS // BR
NT = BLOCKS // 2
TILES = IMAGES * NT
CONVS = 6
WIDTH = PAIRS + 4
HIDDEN = 32
EPS = 1e-6
UNROLL = 4
XRING, ARING, ORING, PRING = 4, 2, 2, 4

FIRST = [(c + 1) // 2 for c in range(CONVS)]
LAST = [(2 * TILES - 1 + c + 1) // 2 for c in range(CONVS)]
STEPS = LAST[5] + CONVS
RAMP = 3 * UNROLL
TOP_Q, BOTTOM_Q = slice(0, QUAD), slice(QUAD, 2 * QUAD)
FIRST_ROW, LAST_ROW = slice(0, QUAD), slice((BR - 1) * QUAD, BR * QUAD)


def conv_kernel(nc, x, weights, conv_bias, w1, b1, w2, out_bias, scalars, distance, row_index,
                edge, out):
    table = nc.dram_tensor("position_bias", (NT, P, 2, PAIRS), F32, kind="Internal").ap()

    with ExitStack() as ctx:
        def sb(name, shape, dt=F32):
            return ctx.enter_context(nc.sbuf_tensor(name, shape, dt))

        def sem(name):
            return ctx.enter_context(nc.semaphore(name))

        w_raw = sb("w_raw", [P, CONVS, 3, P])
        w_high = sb("w_high", [P, CONVS, 3, P], F32R)
        w_low = sb("w_low", [P, CONVS, 3, P], F32R)
        bias_sb = sb("conv_bias_sb", [P, CONVS])
        edge_sb = sb("edge_sb", [P, 2, 2])
        zeros = sb("zeros", [P, 2, WIDTH])
        resid = {L: sb(f"resid{L}", [P, XRING, 2, PAIRS]) for L in (0, 2, 4)}
        relu = {L: sb(f"relu{L}", [P, 2, PAIRS + 1]) for L in (1, 3, 5)}
        split = [sb(f"split{L}", [P, 2, 2 * ARING, WIDTH], F32R) for L in range(CONVS)]
        halo = [sb(f"halo{L}", [P, 2, 2, WIDTH], F32R) for L in range(CONVS)]
        pos_tile = sb("pos_tile", [P, ORING, 2, PAIRS])
        out_tile = sb("out_tile", [P, ORING, 2, PAIRS])
        pos_new = sb("pos_new", [P, 2, 2, PAIRS])
        dist_sb = sb("dist_sb", [P, 2, 2 * PAIRS])
        row_sb = sb("row_sb", [P, 2, BLOCKS])
        w2_sb = sb("w2_sb", [P, 2, P])
        small = sb("small", [P, 6])
        magnitude = sb("magnitude", [P, 3])
        hidden = sb("hidden", [P, 2, 2, 2, PAIRS])
        ps = ctx.enter_context(nc.psum_tensor("ps", [P, 8, 2 * PAIRS], F32))
        pos_sums = [ps[:, 6 + k, :].rearrange("p (b w) -> p b w", b=2) for k in range(2)]

        consts_in, weights_in = sem("consts_in"), sem("weights_in")
        w_high_made, w_low_made, cleared = sem("w_high_made"), sem("w_low_made"), sem("cleared")
        prep_v, prep_a = sem("prep_v"), sem("prep_a")
        hidden_made, pos_summed = sem("hidden_made"), sem("pos_summed")
        pos_made, pos_stored = sem("pos_made"), [sem(f"pos_stored{i}") for i in range(2)]
        x_in = [sem(f"x_in{i}") for i in range(XRING)]
        pos_in = [sem(f"pos_in{i}") for i in range(ORING)]
        out_stored = [sem(f"out_stored{i}") for i in range(ORING)]
        conv_done = [sem(f"conv_done{c}") for c in range(CONVS)]
        level_made = [None] + [sem(f"level_made{L}") for L in range(1, CONVS + 1)]
        edges_cut = {L: sem(f"edges_cut{L}") for L in (1, 3, 5)}
        high_made = [sem(f"high_made{L}") for L in range(CONVS)]
        low_made = [sem(f"low_made{L}") for L in range(CONVS)]
        top_in = [sem(f"top_in{L}") for L in range(CONVS)]
        bottom_in = [sem(f"bottom_in{L}") for L in range(CONVS)]
        halo_made = [sem(f"halo_made{L}") for L in range(CONVS)]
        out_made = sem("out_made")

        block = ctx.enter_context(nc.Block())

        def conv_runs(c, t):
            return not isinstance(t, int) or FIRST[c] <= t <= LAST[c]

        def level_has(L, u):
            return (not isinstance(u, int) or 0 <= u < TILES) if L == 0 else conv_runs(L - 1, u)

        def nth(L, u):
            return u + 1 if L == 0 else u - FIRST[L - 1] + 1

        def nth_conv(c, t):
            return t - FIRST[c] + 1

        def banks(c, phase):
            turn = (CONVS * phase + CONVS - 1 - c) % PRING
            first = (0, 1, 3, 4)[turn]
            if c % 2:
                return ps[:, first, :].rearrange("p (b w) -> p b w", b=2)
            return ps[:, first:first + 2, 0:PAIRS + 2]

        def blocks(n):
            return slice(2 * (n % ARING), 2 * (n % ARING) + 2)

        def steps(engine, step):
            for s in range(RAMP):
                step(s, s % UNROLL, s // 2, True)
            for start, end in ((RAMP, NT), (NT, TILES - UNROLL)):
                with engine.Fori(start // UNROLL, end // UNROLL) as i:
                    for k in range(UNROLL):
                        step(i * UNROLL + k, k, i * (UNROLL // 2) + k // 2, end == NT)
            for s in range(TILES - UNROLL, STEPS):
                step(s, s % UNROLL, s // 2, False)

        @block.sync
        def _(sp):
            sp.dma_start(w_raw[:, :, :, :], weights).then_inc(weights_in, 16)
            for dst, src in ((dist_sb[:, :, :], distance), (row_sb[:, :, :], row_index),
                             (w2_sb[:, :, :], w2), (small[:, 0:1], w1), (small[:, 1:2], b1),
                             (small[:, 2:3], out_bias), (small[:, 3:6], scalars),
                             (bias_sb[:, :], conv_bias), (edge_sb[:, :, :], edge)):
                sp.dma_start(dst, src).then_inc(consts_in, 16)
            for u in range(XRING):
                sp.dma_start(resid[0][:, u, :, :], x[u]).then_inc(x_in[u], 16)

            sp.wait_ge(cleared, 2)

            def top(L, s, phase, j):
                u = s + 1 - L
                if not conv_runs(L, u):
                    return
                if conv_runs(L, u - 1):
                    sp.wait_ge(conv_done[L], nth_conv(L, u - 1))
                elif level_has(L, u - 1):
                    sp.wait_ge(low_made[L], nth(L, u - 1))
                src = split[L][LAST_ROW, :, blocks(phase - L), :].bitcast(F32)
                dst = halo[L][TOP_Q, :, :, :].bitcast(F32)
                if j is not None and (j + 1 - L) % NT == (L + 1) // 2:
                    cut = 1 - L % 2
                    sp.dma_start(dst[:, :, cut, :], zeros[TOP_Q, :, :]).then_inc(top_in[L], 16)
                    sp.dma_start(dst[:, :, 1 - cut, :], src[:, :, 1 - cut, :]).then_inc(top_in[L], 16)
                else:
                    sp.dma_start(dst, src).then_inc(top_in[L], 32)

            def bottom(L, s, phase, j):
                u = s + 1 - L
                if not conv_runs(L, u):
                    return
                if level_has(L, u):
                    sp.wait_ge(low_made[L], nth(L, u))
                elif conv_runs(L, u - 1):
                    sp.wait_ge(conv_done[L], nth_conv(L, u - 1))
                src = split[L][FIRST_ROW, :, blocks(phase + 1 - L), :].bitcast(F32)
                dst = halo[L][BOTTOM_Q, :, :, :].bitcast(F32)
                if j is not None and (j + 1 - L) % NT == L // 2:
                    cut = L % 2
                    sp.dma_start(dst[:, :, cut, :], zeros[BOTTOM_Q, :, :]).then_inc(bottom_in[L], 16)
                    sp.dma_start(dst[:, :, 1 - cut, :], src[:, :, 1 - cut, :]).then_inc(bottom_in[L], 16)
                else:
                    sp.dma_start(dst, src).then_inc(bottom_in[L], 32)

            def step(s, phase, j, half, table_tile, first):
                static = isinstance(s, int)
                before = None if j is None else j - 1
                for c in reversed(range(CONVS)):
                    top(c, s, phase, j)
                    if c + 2 < CONVS:
                        bottom(c + 2, s, phase, j)
                    else:
                        bottom(c - 4, s - 1, phase - 1, before)
                    if c == 5 and (not static or CONVS + 1 <= s < STEPS - 1):
                        if not static or s - CONVS - 1 >= ORING:
                            sp.wait_ge(out_made, s - (CONVS + 2))
                        n = (j - CONVS - 1) % NT if j is not None else table_tile
                        if first:
                            sp.wait_ge(pos_stored[(phase + 1) % 2], (half - (CONVS // 2 - phase % 2)) * 16)
                        sp.dma_start(pos_tile[:, (phase + 1) % ORING, :, :], table[n]).then_inc(
                            pos_in[(phase + 1) % ORING], 16)
                    if c == 4 and conv_runs(5, s - 5):
                        sp.wait_ge(out_made, nth_conv(5, s - 5))
                        sp.dma_start(out[s - 8], out_tile[:, phase % ORING, :, :]).then_inc(
                            out_stored[phase % ORING], 16)
                    if c == 0 and first:
                        sp.wait_ge(pos_made, s + 1)
                        sp.dma_start(table[s], pos_new[:, phase % 2, :, :]).then_inc(
                            pos_stored[phase % 2], 16)
                    if c == 0 and (not static or XRING <= s + 2 < TILES):
                        sp.wait_ge(level_made[2], nth(2, s - 1))
                        sp.dma_start(resid[0][:, (phase + 2) % XRING, :, :], x[s + 2]).then_inc(
                            x_in[(phase + 2) % XRING], 16)

            def edge_steps(base, places, first=False):
                for j in places:
                    step(base + j, j % UNROLL, j, (base + j) // 2 if first else None, None, first)

            def middle(base, groups, first=False):
                with sp.Fori(RAMP // UNROLL, groups) as i:
                    for k in range(UNROLL):
                        step(base + i * UNROLL + k, k, None, i * (UNROLL // 2) + k // 2,
                             i * UNROLL + (k - CONVS - 1), first)

            top(0, -1, UNROLL - 1, NT - 1)
            edge_steps(0, range(RAMP), True)
            middle(0, NT // UNROLL - 1, True)
            edge_steps(0, range(NT - UNROLL, NT), True)
            for k in range(2):
                sp.wait_ge(pos_stored[k], 16 * (NT // 2))
            with sp.Fori(1, IMAGES - 1) as image:
                edge_steps(image * NT, range(RAMP))
                middle(image * NT, NT // UNROLL - 1)
                edge_steps(image * NT, range(NT - UNROLL, NT))
            edge_steps(TILES - NT, range(RAMP))
            middle(TILES - NT, NT // UNROLL - 1)
            for s in range(TILES - UNROLL, STEPS):
                step(s, s % UNROLL, s % NT, None, None, False)
            for k in range(ORING):
                sp.wait_ge(out_stored[k], 16 * (TILES // ORING))

        @block.tensor
        def _(pe):
            def second_layer(T, k):
                pe.wait_ge(hidden_made, T + 1)
                if not isinstance(T, int) or T >= 2:
                    pe.wait_ge(pos_made, T - 1)
                for g in range(2):
                    mm = pe.matmul(pos_sums[k], w2_sb[:, g, :], hidden[:, k, g, :, :],
                                   start=(g == 0), stop=(g == 1))
                mm.then_inc(pos_summed, 1)

            pe.wait_ge(consts_in, 16 * 9)
            pe.wait_ge(w_low_made, 1)

            def conv(c, s, phase):
                t = s - c
                if not conv_runs(c, t):
                    return
                if level_has(c, t):
                    pe.wait_ge(low_made[c], nth(c, t))
                before, at = c, s
                for _ in range(3):
                    before, at = (before + 4, at) if before < 2 else (before - 2, at - 1)
                    if conv_runs(before, at - before):
                        pe.wait_ge(level_made[before + 1], nth_conv(before, at - before))
                        break
                ring = [(2 * (phase - c) - 1) % (2 * ARING), 2 * (phase - c) % (2 * ARING)]
                sums = banks(c, phase)
                products = ((0, w_high), (0, w_low), (1, w_high))
                if c % 2:
                    both = slice(ring[0], ring[1] + 1) if ring[0] < ring[1] else slice(ring[0], None, -ring[0])
                    for shift in range(2):
                        for k, (part, w) in enumerate(products):
                            pe.matmul(sums, w[:, c, shift, :], split[c][:, part, both, shift:shift + PAIRS],
                                      start=(shift == 0 and k == 0), stop=False)
                else:
                    for shift in range(2):
                        for k, (part, w) in enumerate(products):
                            for b in range(2):
                                pe.matmul(sums[:, b, :], w[:, c, shift, :],
                                          split[c][:, part, ring[b], shift:shift + PAIRS + 2],
                                          start=(shift == 0 and k == 0), stop=False)
                pe.wait_ge(halo_made[c], nth_conv(c, t))
                for k, (part, w) in enumerate(products):
                    if c % 2:
                        mm = pe.matmul(sums, w[:, c, 2, :], halo[c][:, part, :, 0:PAIRS],
                                       start=False, stop=(k == 2))
                    else:
                        for b in range(2):
                            mm = pe.matmul(sums[:, b, :], w[:, c, 2, :], halo[c][:, part, b, 0:PAIRS + 2],
                                           start=False, stop=(k == 2))
                mm.then_inc(conv_done[c], 1)

            def step(s, phase, half, first):
                for c in reversed(range(CONVS)):
                    conv(c, s, phase)
                    if c == 2 and first:
                        second_layer(s, phase % 2)

            steps(pe, step)

        @block.gpsimd
        def _(pool):
            for L in range(1, CONVS):
                last = nc.gpsimd.memset(split[L][:, :, :, :].bitcast(F32), 0.0)
            last.then_inc(cleared, 1)

        @block.scalar
        def _(act):
            act.wait_ge(weights_in, 16)
            nc.scalar.activation(w_high[:, :, :, :], w_raw[:, :, :, :], ACT.Copy).then_inc(w_high_made, 1)
            act.wait_ge(prep_v, 5)
            nc.scalar.activation(dist_sb[:, :, :], dist_sb[:, :, :], ACT.Ln, bias=1.0).then_inc(prep_a, 1)
            nc.scalar.activation(row_sb[:, :, :], row_sb[:, :, :], ACT.Ln, bias=1.0).then_inc(prep_a, 1)
            act.wait_ge(prep_v, 8)

            def hidden_tile(T, k):
                if not isinstance(T, int) or T >= 2:
                    act.wait_ge(pos_summed, T - 1)
                for b in range(2):
                    for g in range(2):
                        h = nc.scalar.activation(
                            hidden[:, k, g, b, :],
                            dist_sb[:, g, bass.ds(2 * (BLOCKS - 1) - (T * 4 + 2 * b), PAIRS)],
                            ACT.Relu, bias=small[:, 1:2],
                            scale=row_sb[:, g, bass.ds(T * 2 + b, 1)])
                h.then_inc(hidden_made, 1)

            def split_input(u, phase):
                if not level_has(0, u):
                    return
                act.wait_ge(x_in[phase % XRING], load_count(u, phase))
                if conv_runs(0, u - 1):
                    act.wait_ge(conv_done[0], nth_conv(0, u - 1))
                nc.scalar.activation(split[0][:, 0, blocks(phase), 1:PAIRS + 1],
                                     resid[0][:, phase % XRING, :, :], ACT.Copy).then_inc(high_made[0], 1)

            def load_count(u, phase):
                return 16 * (u // XRING + 1) if isinstance(u, int) else (u - phase % XRING) * 4 + 16

            def shift_halo(L, u):
                if not conv_runs(L, u):
                    return
                act.wait_ge(top_in[L], nth_conv(L, u) * 32)
                act.wait_ge(bottom_in[L], nth_conv(L, u) * 32)
                nc.scalar.activation(
                    halo[L][64:128, :, :, 0:WIDTH - 1].rearrange("p h b w -> p (h b) w"),
                    halo[L][0:64, :, :, 1:WIDTH].rearrange("p h b w -> p (h b) w").bitcast(F32),
                    ACT.Copy).then_inc(halo_made[L], 1)

            def step(s, phase, half, first):
                for c in reversed(range(CONVS)):
                    if c == 5 and first:
                        hidden_tile(s, phase % 2)
                    if c % 2 == 0 and conv_runs(c, s - c):
                        L = c + 1
                        act.wait_ge(conv_done[c], nth_conv(c, s - c))
                        if conv_runs(c, s - c - 1):
                            act.wait_ge(low_made[L], nth_conv(c, s - c - 1))
                        nc.scalar.activation(relu[L][:, :, :], banks(c, phase)[:, :, 0:PAIRS + 1], ACT.Relu,
                                             bias=bias_sb[:, c:c + 1]).then_inc(level_made[L], 1)
                    if c == 0:
                        split_input(s + 1, phase + 1)
                    if c + 3 < CONVS:
                        shift_halo(c + 3, s - c - 2)
                    else:
                        shift_halo(c - 3, s - c + 3)

            act.wait_ge(cleared, 2)
            split_input(0, 0)
            steps(act, step)

        @block.vector
        def _(dve):
            nc.vector.memset(zeros[:, :, :], 0.0)
            nc.vector.memset(split[0][:, :, :, :].bitcast(F32), 0.0).then_inc(cleared, 1)
            dve.wait_ge(cleared, 2)
            dve.wait_ge(consts_in, 16 * 9)
            product, abs_c, threshold = magnitude[:, 0:1], magnitude[:, 1:2], magnitude[:, 2:3]
            nc.vector.tensor_tensor(product, small[:, 4:5], small[:, 5:6], ALU.mult).then_inc(prep_v, 1)
            nc.vector.scalar_tensor_tensor(out=abs_c, in0=small[:, 3:4], scalar=-1.0, in1=small[:, 3:4],
                                           op0=ALU.mult, op1=ALU.max).then_inc(prep_v, 1)
            dve.wait_ge(prep_v, 2)
            nc.vector.scalar_tensor_tensor(out=threshold, in0=product, scalar=-1.0, in1=product,
                                           op0=ALU.mult, op1=ALU.max).then_inc(prep_v, 1)
            nc.vector.tensor_scalar(dist_sb[:, :, :], dist_sb[:, :, :], abs_c, None,
                                    ALU.mult).then_inc(prep_v, 1)
            dve.wait_ge(prep_v, 3)
            nc.vector.tensor_scalar(row_sb[:, :, :], row_sb[:, :, :], threshold, abs_c,
                                    ALU.max, ALU.mult).then_inc(prep_v, 1)
            dve.wait_ge(prep_a, 2)
            nc.vector.tensor_scalar(row_sb[:, :, :], row_sb[:, :, :], EPS, None, ALU.add).then_inc(prep_v, 1)
            dve.wait_ge(prep_v, 6)
            nc.vector.reciprocal(row_sb[:, :, :], row_sb[:, :, :]).then_inc(prep_v, 1)
            dve.wait_ge(prep_v, 7)
            nc.vector.tensor_scalar(row_sb[:, :, :], row_sb[:, :, :], small[:, 0:1], None,
                                    ALU.mult).then_inc(prep_v, 1)
            dve.wait_ge(w_high_made, 1)
            nc.vector.tensor_tensor(w_low[:, :, :, :], w_raw[:, :, :, :], w_high[:, :, :, :].bitcast(F32),
                                    ALU.subtract).then_inc(w_low_made, 1)

            def table_tile(T, k, half):
                dve.wait_ge(pos_summed, T + 1)
                if not isinstance(T, int) or T >= 2:
                    dve.wait_ge(pos_stored[k], half * 16)
                nc.vector.tensor_scalar(pos_new[:, k, :, :], pos_sums[k], small[:, 2:3], None,
                                        ALU.add).then_inc(pos_made, 1)

            def low(L, phase, src, dst_cols):
                nc.vector.tensor_tensor(
                    split[L][:, 1, blocks(phase), dst_cols], src,
                    split[L][:, 0, blocks(phase), dst_cols].bitcast(F32), ALU.subtract
                ).then_inc(low_made[L], 1)

            def relu_level(L, s, phase):
                u, c = s + 1 - L, L - 1
                if not conv_runs(c, u):
                    return
                dve.wait_ge(level_made[L], nth(L, u))
                ends = relu[L][:, :, 0:PAIRS + 1:PAIRS]
                nc.vector.tensor_tensor(ends, ends, edge_sb[:, :, :], ALU.min).then_inc(edges_cut[L], 1)
                if L < CONVS and conv_runs(L, s - L):
                    dve.wait_ge(conv_done[L], nth_conv(L, s - L))
                dve.wait_ge(edges_cut[L], nth(L, u))
                nc.vector.tensor_copy(split[L][:, 0, blocks(phase + 1 - L), 0:PAIRS + 1],
                                      relu[L][:, :, :]).then_inc(high_made[L], 1)
                dve.wait_ge(high_made[L], nth(L, u))
                low(L, phase + 1 - L, relu[L][:, :, :], slice(0, PAIRS + 1))

            def residual_level(L, s, phase):
                u, c = s + 1 - L, L - 1
                if not conv_runs(c, u):
                    return
                dve.wait_ge(conv_done[c], nth(L, u))
                slot = (phase + 1 - L) % XRING
                if L == 2:
                    dve.wait_ge(high_made[0], nth(0, u - 1))
                    dve.wait_ge(low_made[0], nth(0, u - 1))
                else:
                    dve.wait_ge(level_made[L - 2], nth(L - 2, u - 1))
                nc.vector.scalar_tensor_tensor(
                    out=resid[L][:, slot, :, :], in0=banks(c, phase),
                    scalar=bias_sb[:, c:c + 1], in1=resid[L - 2][:, (slot - 1) % XRING, :, :],
                    op0=ALU.add, op1=ALU.add).then_inc(level_made[L], 1)
                if conv_runs(L, s - L):
                    dve.wait_ge(conv_done[L], nth_conv(L, s - L))
                dve.wait_ge(level_made[L], nth(L, u))
                nc.vector.tensor_copy(split[L][:, 0, blocks(phase + 1 - L), 1:PAIRS + 1],
                                      resid[L][:, slot, :, :]).then_inc(high_made[L], 1)
                dve.wait_ge(high_made[L], nth(L, u))
                low(L, phase + 1 - L, resid[L][:, slot, :, :], slice(1, PAIRS + 1))

            def result(s, phase, pairs_before):
                u = s - 5
                if not conv_runs(5, u):
                    return
                dve.wait_ge(conv_done[5], nth_conv(5, u))
                dve.wait_ge(level_made[4], nth(4, u - 1))
                if pairs_before is not None:
                    dve.wait_ge(out_stored[phase % ORING], pairs_before * 16)
                tile = out_tile[:, phase % ORING, :, :]
                nc.vector.scalar_tensor_tensor(
                    out=tile, in0=banks(5, phase), scalar=bias_sb[:, 5:6],
                    in1=resid[4][:, (phase - 6) % XRING, :, :], op0=ALU.add, op1=ALU.add
                ).then_inc(level_made[6], 1)

            def add_position(s, phase, nth_load):
                u = s - 5
                if not conv_runs(5, u):
                    return
                tile = out_tile[:, phase % ORING, :, :]
                dve.wait_ge(pos_in[phase % ORING], nth_load * 16)
                dve.wait_ge(level_made[6], nth(6, u))
                nc.vector.tensor_tensor(tile, tile, pos_tile[:, phase % ORING, :, :], ALU.add).then_inc(out_made, 1)

            def step(s, phase, half, first):
                n = half - 4
                result(s, phase, n if not isinstance(n, int) or n > 0 else None)
                add_position(s, phase, n + 1)
                relu_level(5, s, phase)
                residual_level(4, s, phase)
                relu_level(3, s, phase)
                if first:
                    table_tile(s, phase % 2, half)
                residual_level(2, s, phase)
                relu_level(1, s, phase)
                if level_has(0, s + 1):
                    dve.wait_ge(high_made[0], nth(0, s + 1))
                    low(0, phase + 1, resid[0][:, (phase + 1) % XRING, :, :], slice(1, PAIRS + 1))

            dve.wait_ge(high_made[0], 1)
            low(0, 0, resid[0][:, 0, :, :], slice(1, PAIRS + 1))
            steps(dve, step)


def band(w):
    w = np.transpose(w, (2, 3, 1, 0))
    m = np.zeros((3, BR, BC, CH, BR, BC, CH), w.dtype)
    h = m[2].reshape(2, 2, BC, CH, BR, BC, CH)
    for shift in range(2):
        for ci in range(BC):
            for co in range(BC):
                dx = ci - co + 2 * shift
                if not 0 <= dx <= 2:
                    continue
                for ro in range(BR):
                    for ri in range(max(0, ro - 1), min(BR, ro + 2)):
                        m[shift, ri, ci, :, ro, co, :] = w[ri - ro + 1, dx]
                h[shift, 0, ci, :, 0, co, :] = w[0, dx]
                h[shift, 1, ci, :, BR - 1, co, :] = w[2, dx]
    return m.reshape(3, P, P).transpose(1, 0, 2)


def kernel(**inputs):
    import concourse.bacc as bacc
    from concourse.bass_utils import run_bass_kernel_spmd

    a = {k: np.asarray(v) for k, v in inputs.items()}
    f32 = np.float32

    def tiled(v):
        v = v.reshape(IMAGES, CH, NT, 2, BR, PAIRS, BC).transpose(0, 2, 4, 6, 1, 3, 5)
        return np.ascontiguousarray(v).reshape(TILES, P, 2, PAIRS)

    convs = [(a[f"L{n}_conv_w{i}"], a[f"L{n}_conv_b{i}"]) for n in range(3) for i in (1, 2)]
    pixels = 4
    w2 = np.zeros((2, BC, HIDDEN, 2, BR, BC, CH), f32)
    for g in range(2):
        for r in range(2):
            for c in range(BC):
                w2[r, c, :, g, 2 * g + r, c, :] = a["L3_conv_W2"]
    m = np.arange(2 * PAIRS)
    r, c, g = np.arange(2)[:, None, None, None], np.arange(BC)[:, None, None], np.arange(2)[:, None]
    distance = np.maximum(2 * (2 * (BLOCKS - 1) - m) + 2 * g + r - c, 0)
    distance = np.repeat(distance.reshape(pixels, 1, 2, 2 * PAIRS), HIDDEN, 1)
    rows = BR * np.arange(BLOCKS) + 2 * g + r + 0 * c
    rows = np.repeat(rows.reshape(pixels, 1, 2, BLOCKS), HIDDEN, 1)
    edge = np.full((BR, BC, CH, 2, 2), np.finfo(f32).max, f32)
    edge[:, 0, :, :, 0] = 0
    edge[:, 1, :, :, 1] = 0
    arrays = {
        "x": tiled(a["x"]),
        "weights": np.stack([band(w) for w, _ in convs], 1),
        "conv_bias": np.stack([np.tile(b, BR * BC) for _, b in convs], 1),
        "w1": np.tile(a["L3_conv_W1"].reshape(HIDDEN), pixels).reshape(P, 1),
        "b1": np.tile(a["L3_conv_b1"], pixels).reshape(P, 1),
        "w2": w2.reshape(P, 2, P),
        "out_bias": np.tile(a["L3_conv_b2"], BR * BC).reshape(P, 1),
        "scalars": np.tile(np.stack([a["L3_conv_c"], a["L3_conv_L_multiplier"], a["L3_conv_init_L"]])
                           .reshape(1, 3), (P, 1)),
        "distance": distance.reshape(P, 2, 2 * PAIRS).astype(f32),
        "row_index": rows.reshape(P, 2, BLOCKS).astype(f32),
        "edge": edge.reshape(P, 2, 2),
    }
    nc = bacc.Bacc("TRN2", target_bir_lowering=False, num_devices=1)
    aps = {}
    for name, v in arrays.items():
        arrays[name] = v = np.ascontiguousarray(v)
        aps[name] = nc.dram_tensor(name, v.shape, mybir.dt.from_np(v.dtype), kind="ExternalInput").ap()
    out = nc.dram_tensor("out", (TILES, P, 2, PAIRS), F32, kind="ExternalOutput").ap()
    conv_kernel(nc, out=out, **aps)
    result = run_bass_kernel_spmd(nc, [arrays], core_ids=[0]).results[0]["out"]
    result = np.asarray(result).reshape(IMAGES, NT, BR, BC, CH, 2, PAIRS).transpose(0, 4, 1, 5, 2, 6, 3)
    return result.reshape(1, IMAGES, CH, ROWS, COLS)[0]
```
